# Optimizing a Trainium2 kernel written in Bass

```python
import numpy as np
import jax
import jax.numpy as jnp

def _softmax(x, axis=-1):
    return jax.nn.softmax(x, axis=axis)

def _gelu(x):
    return jax.nn.gelu(x, approximate=True)

def _silu(x):
    return jax.nn.silu(x)

def _sigmoid(x):
    return jax.nn.sigmoid(x)

def _layernorm(x, axis=-1, eps=1e-05):
    m = jnp.mean(x, axis=axis, keepdims=True)
    v = jnp.var(x, axis=axis, keepdims=True)
    return (x - m) / jnp.sqrt(v + eps)

def _scatter_add(tgt, idx, src, axis=0):
    return tgt.at[idx].add(src)

def _segment_sum(src, seg, n):
    return jax.ops.segment_sum(src, seg, n)
kernel_name = 'mk_dlrm_tower_d1_rec_r8_9a5cf5'

def setup_inputs(seed: int=0):
    np.random.seed(seed)
    _w = jnp.asarray

    def _rec_inputs():
        import jax
        import jax.numpy as jnp
        _tk = jax.random.key(seed)
        dense_ctx = jax.random.normal(jax.random.fold_in(_tk, 190), (512, 16), jnp.float32)
        ids = jnp.stack([jax.random.randint(jax.random.fold_in(_tk, 200 + f), (512,), 0, v, jnp.int32) for f, v in enumerate([125000, 1250, 1000, 1000, 125000, 1250, 1250, 1250, 1250, 12500, 1000, 1250, 1250, 1250, 1000, 12500, 12500, 125000, 1000, 12500, 125000, 125000, 12500, 1250, 1000, 1000, 1000, 12500, 1000, 12500, 1250, 125000, 1250, 12500, 1250, 1000, 1250, 12500, 1250, 1250, 1000, 1000, 12500, 1000, 12500, 1000, 1250, 1000])], axis=1)
        tbl_0 = 0.05 * jax.random.normal(jax.random.fold_in(_tk, 500 + 0), (125000, 32), jnp.float32)
        tbl_1 = 0.05 * jax.random.normal(jax.random.fold_in(_tk, 500 + 1), (1250, 32), jnp.float32)
        tbl_2 = 0.05 * jax.random.normal(jax.random.fold_in(_tk, 500 + 2), (1000, 32), jnp.float32)
        tbl_3 = 0.05 * jax.random.normal(jax.random.fold_in(_tk, 500 + 3), (1000, 32), jnp.float32)
        tbl_4 = 0.05 * jax.random.normal(jax.random.fold_in(_tk, 500 + 4), (125000, 32), jnp.float32)
        tbl_5 = 0.05 * jax.random.normal(jax.random.fold_in(_tk, 500 + 5), (1250, 32), jnp.float32)
        tbl_6 = 0.05 * jax.random.normal(jax.random.fold_in(_tk, 500 + 6), (1250, 32), jnp.float32)
        tbl_7 = 0.05 * jax.random.normal(jax.random.fold_in(_tk, 500 + 7), (1250, 32), jnp.float32)
        tbl_8 = 0.05 * jax.random.normal(jax.random.fold_in(_tk, 500 + 8), (1250, 32), jnp.float32)
        tbl_9 = 0.05 * jax.random.normal(jax.random.fold_in(_tk, 500 + 9), (12500, 32), jnp.float32)
        tbl_10 = 0.05 * jax.random.normal(jax.random.fold_in(_tk, 500 + 10), (1000, 32), jnp.float32)
        tbl_11 = 0.05 * jax.random.normal(jax.random.fold_in(_tk, 500 + 11), (1250, 32), jnp.float32)
        tbl_12 = 0.05 * jax.random.normal(jax.random.fold_in(_tk, 500 + 12), (1250, 32), jnp.float32)
        tbl_13 = 0.05 * jax.random.normal(jax.random.fold_in(_tk, 500 + 13), (1250, 32), jnp.float32)
        tbl_14 = 0.05 * jax.random.normal(jax.random.fold_in(_tk, 500 + 14), (1000, 32), jnp.float32)
        tbl_15 = 0.05 * jax.random.normal(jax.random.fold_in(_tk, 500 + 15), (12500, 32), jnp.float32)
        tbl_16 = 0.05 * jax.random.normal(jax.random.fold_in(_tk, 500 + 16), (12500, 32), jnp.float32)
        tbl_17 = 0.05 * jax.random.normal(jax.random.fold_in(_tk, 500 + 17), (125000, 32), jnp.float32)
        tbl_18 = 0.05 * jax.random.normal(jax.random.fold_in(_tk, 500 + 18), (1000, 32), jnp.float32)
        tbl_19 = 0.05 * jax.random.normal(jax.random.fold_in(_tk, 500 + 19), (12500, 32), jnp.float32)
        tbl_20 = 0.05 * jax.random.normal(jax.random.fold_in(_tk, 500 + 20), (125000, 32), jnp.float32)
        tbl_21 = 0.05 * jax.random.normal(jax.random.fold_in(_tk, 500 + 21), (125000, 32), jnp.float32)
        tbl_22 = 0.05 * jax.random.normal(jax.random.fold_in(_tk, 500 + 22), (12500, 32), jnp.float32)
        tbl_23 = 0.05 * jax.random.normal(jax.random.fold_in(_tk, 500 + 23), (1250, 32), jnp.float32)
        tbl_24 = 0.05 * jax.random.normal(jax.random.fold_in(_tk, 500 + 24), (1000, 32), jnp.float32)
        tbl_25 = 0.05 * jax.random.normal(jax.random.fold_in(_tk, 500 + 25), (1000, 32), jnp.float32)
        tbl_26 = 0.05 * jax.random.normal(jax.random.fold_in(_tk, 500 + 26), (1000, 32), jnp.float32)
        tbl_27 = 0.05 * jax.random.normal(jax.random.fold_in(_tk, 500 + 27), (12500, 32), jnp.float32)
        tbl_28 = 0.05 * jax.random.normal(jax.random.fold_in(_tk, 500 + 28), (1000, 32), jnp.float32)
        tbl_29 = 0.05 * jax.random.normal(jax.random.fold_in(_tk, 500 + 29), (12500, 32), jnp.float32)
        tbl_30 = 0.05 * jax.random.normal(jax.random.fold_in(_tk, 500 + 30), (1250, 32), jnp.float32)
        tbl_31 = 0.05 * jax.random.normal(jax.random.fold_in(_tk, 500 + 31), (125000, 32), jnp.float32)
        tbl_32 = 0.05 * jax.random.normal(jax.random.fold_in(_tk, 500 + 32), (1250, 32), jnp.float32)
        tbl_33 = 0.05 * jax.random.normal(jax.random.fold_in(_tk, 500 + 33), (12500, 32), jnp.float32)
        tbl_34 = 0.05 * jax.random.normal(jax.random.fold_in(_tk, 500 + 34), (1250, 32), jnp.float32)
        tbl_35 = 0.05 * jax.random.normal(jax.random.fold_in(_tk, 500 + 35), (1000, 32), jnp.float32)
        tbl_36 = 0.05 * jax.random.normal(jax.random.fold_in(_tk, 500 + 36), (1250, 32), jnp.float32)
        tbl_37 = 0.05 * jax.random.normal(jax.random.fold_in(_tk, 500 + 37), (12500, 32), jnp.float32)
        tbl_38 = 0.05 * jax.random.normal(jax.random.fold_in(_tk, 500 + 38), (1250, 32), jnp.float32)
        tbl_39 = 0.05 * jax.random.normal(jax.random.fold_in(_tk, 500 + 39), (1250, 32), jnp.float32)
        tbl_40 = 0.05 * jax.random.normal(jax.random.fold_in(_tk, 500 + 40), (1000, 32), jnp.float32)
        tbl_41 = 0.05 * jax.random.normal(jax.random.fold_in(_tk, 500 + 41), (1000, 32), jnp.float32)
        tbl_42 = 0.05 * jax.random.normal(jax.random.fold_in(_tk, 500 + 42), (12500, 32), jnp.float32)
        tbl_43 = 0.05 * jax.random.normal(jax.random.fold_in(_tk, 500 + 43), (1000, 32), jnp.float32)
        tbl_44 = 0.05 * jax.random.normal(jax.random.fold_in(_tk, 500 + 44), (12500, 32), jnp.float32)
        tbl_45 = 0.05 * jax.random.normal(jax.random.fold_in(_tk, 500 + 45), (1000, 32), jnp.float32)
        tbl_46 = 0.05 * jax.random.normal(jax.random.fold_in(_tk, 500 + 46), (1250, 32), jnp.float32)
        tbl_47 = 0.05 * jax.random.normal(jax.random.fold_in(_tk, 500 + 47), (1000, 32), jnp.float32)
        _rk = jax.random.fold_in(_tk, 7)
        W_top1 = 0.0693375 * jax.random.normal(jax.random.fold_in(_tk, 801), (208, 512), jnp.float32)
        W_top2 = 0.0441942 * jax.random.normal(jax.random.fold_in(_tk, 802), (512, 256), jnp.float32)
        W_top3 = 0.0625 * jax.random.normal(jax.random.fold_in(_tk, 803), (256, 1), jnp.float32)
        b_top1 = jnp.zeros((512,), jnp.float32)
        b_top2 = jnp.zeros((256,), jnp.float32)
        return (dense_ctx, ids, tbl_0, tbl_1, tbl_2, tbl_3, tbl_4, tbl_5, tbl_6, tbl_7, tbl_8, tbl_9, tbl_10, tbl_11, tbl_12, tbl_13, tbl_14, tbl_15, tbl_16, tbl_17, tbl_18, tbl_19, tbl_20, tbl_21, tbl_22, tbl_23, tbl_24, tbl_25, tbl_26, tbl_27, tbl_28, tbl_29, tbl_30, tbl_31, tbl_32, tbl_33, tbl_34, tbl_35, tbl_36, tbl_37, tbl_38, tbl_39, tbl_40, tbl_41, tbl_42, tbl_43, tbl_44, tbl_45, tbl_46, tbl_47, W_top1, b_top1, W_top2, b_top2, W_top3)
    dense_ctx, ids, tbl_0, tbl_1, tbl_2, tbl_3, tbl_4, tbl_5, tbl_6, tbl_7, tbl_8, tbl_9, tbl_10, tbl_11, tbl_12, tbl_13, tbl_14, tbl_15, tbl_16, tbl_17, tbl_18, tbl_19, tbl_20, tbl_21, tbl_22, tbl_23, tbl_24, tbl_25, tbl_26, tbl_27, tbl_28, tbl_29, tbl_30, tbl_31, tbl_32, tbl_33, tbl_34, tbl_35, tbl_36, tbl_37, tbl_38, tbl_39, tbl_40, tbl_41, tbl_42, tbl_43, tbl_44, tbl_45, tbl_46, tbl_47, W_top1, b_top1, W_top2, b_top2, W_top3 = _rec_inputs()

    def _L0_rec_setup():
        import jax, jax.numpy as jnp
        import numpy as np
        B, F, K, C = (256, 48, 32, 128)
        key = jax.random.key(seed)
        k0, k1, k2 = jax.random.split(key, 3)
        x = jax.random.normal(k0, (B, F, K), dtype=jnp.float32)
        W0 = jax.random.normal(k1, (F * F, C), dtype=jnp.float32) * 0.02
        b0 = jnp.zeros((C,), dtype=jnp.float32)
        W1 = jax.random.normal(k2, (F * (C // 2), C), dtype=jnp.float32) * 0.02
        b1 = jnp.zeros((C,), dtype=jnp.float32)
        return {'x': x, 'W0': W0, 'b0': b0, 'W1': W1, 'b1': b1}
    _L0_rec_all = _L0_rec_setup()
    _L0_rec_in = {k: v for k, v in _L0_rec_all.items() if k in ('W0', 'b0', 'W1', 'b1')}
    del _L0_rec_all
    return {'dense_ctx': dense_ctx, 'ids': ids, 'tbl_0': tbl_0, 'tbl_1': tbl_1, 'tbl_2': tbl_2, 'tbl_3': tbl_3, 'tbl_4': tbl_4, 'tbl_5': tbl_5, 'tbl_6': tbl_6, 'tbl_7': tbl_7, 'tbl_8': tbl_8, 'tbl_9': tbl_9, 'tbl_10': tbl_10, 'tbl_11': tbl_11, 'tbl_12': tbl_12, 'tbl_13': tbl_13, 'tbl_14': tbl_14, 'tbl_15': tbl_15, 'tbl_16': tbl_16, 'tbl_17': tbl_17, 'tbl_18': tbl_18, 'tbl_19': tbl_19, 'tbl_20': tbl_20, 'tbl_21': tbl_21, 'tbl_22': tbl_22, 'tbl_23': tbl_23, 'tbl_24': tbl_24, 'tbl_25': tbl_25, 'tbl_26': tbl_26, 'tbl_27': tbl_27, 'tbl_28': tbl_28, 'tbl_29': tbl_29, 'tbl_30': tbl_30, 'tbl_31': tbl_31, 'tbl_32': tbl_32, 'tbl_33': tbl_33, 'tbl_34': tbl_34, 'tbl_35': tbl_35, 'tbl_36': tbl_36, 'tbl_37': tbl_37, 'tbl_38': tbl_38, 'tbl_39': tbl_39, 'tbl_40': tbl_40, 'tbl_41': tbl_41, 'tbl_42': tbl_42, 'tbl_43': tbl_43, 'tbl_44': tbl_44, 'tbl_45': tbl_45, 'tbl_46': tbl_46, 'tbl_47': tbl_47, 'W_top1': W_top1, 'b_top1': b_top1, 'W_top2': W_top2, 'b_top2': b_top2, 'W_top3': W_top3, 'L0_rec_W0': _L0_rec_in['W0'], 'L0_rec_b0': _L0_rec_in['b0'], 'L0_rec_W1': _L0_rec_in['W1'], 'L0_rec_b1': _L0_rec_in['b1']}

def reference(dense_ctx, ids, tbl_0, tbl_1, tbl_2, tbl_3, tbl_4, tbl_5, tbl_6, tbl_7, tbl_8, tbl_9, tbl_10, tbl_11, tbl_12, tbl_13, tbl_14, tbl_15, tbl_16, tbl_17, tbl_18, tbl_19, tbl_20, tbl_21, tbl_22, tbl_23, tbl_24, tbl_25, tbl_26, tbl_27, tbl_28, tbl_29, tbl_30, tbl_31, tbl_32, tbl_33, tbl_34, tbl_35, tbl_36, tbl_37, tbl_38, tbl_39, tbl_40, tbl_41, tbl_42, tbl_43, tbl_44, tbl_45, tbl_46, tbl_47, W_top1, b_top1, W_top2, b_top2, W_top3, L0_rec_W0, L0_rec_b0, L0_rec_W1, L0_rec_b1):
    import jax
    import jax.numpy as jnp

    def _L0_rec_ref(x, W0, b0, W1, b1):
        import jax, jax.numpy as jnp
        import numpy as np
        B, F, K, C = (256, 48, 32, 128)
        x0 = jnp.transpose(x, (0, 2, 1))
        xk = x0
        results = []
        for i, (W, b) in enumerate(((W0, b0), (W1, b1))):
            fv = xk.shape[2]
            cross = jnp.einsum('bkf,bkg->bkfg', x0, xk).reshape(x.shape[0], K, F * fv)
            z = jax.nn.relu(jnp.einsum('bkc,cd->bkd', cross, W) + b)
            if i != 1:
                xk, direct = jnp.split(z, 2, axis=2)
            else:
                direct = z
            results.append(direct)
        out = jnp.concatenate(results, axis=2).sum(axis=1)
        return out
    e = jnp.stack([tbl_0[ids[:, 0]], tbl_1[ids[:, 1]], tbl_2[ids[:, 2]], tbl_3[ids[:, 3]], tbl_4[ids[:, 4]], tbl_5[ids[:, 5]], tbl_6[ids[:, 6]], tbl_7[ids[:, 7]], tbl_8[ids[:, 8]], tbl_9[ids[:, 9]], tbl_10[ids[:, 10]], tbl_11[ids[:, 11]], tbl_12[ids[:, 12]], tbl_13[ids[:, 13]], tbl_14[ids[:, 14]], tbl_15[ids[:, 15]], tbl_16[ids[:, 16]], tbl_17[ids[:, 17]], tbl_18[ids[:, 18]], tbl_19[ids[:, 19]], tbl_20[ids[:, 20]], tbl_21[ids[:, 21]], tbl_22[ids[:, 22]], tbl_23[ids[:, 23]], tbl_24[ids[:, 24]], tbl_25[ids[:, 25]], tbl_26[ids[:, 26]], tbl_27[ids[:, 27]], tbl_28[ids[:, 28]], tbl_29[ids[:, 29]], tbl_30[ids[:, 30]], tbl_31[ids[:, 31]], tbl_32[ids[:, 32]], tbl_33[ids[:, 33]], tbl_34[ids[:, 34]], tbl_35[ids[:, 35]], tbl_36[ids[:, 36]], tbl_37[ids[:, 37]], tbl_38[ids[:, 38]], tbl_39[ids[:, 39]], tbl_40[ids[:, 40]], tbl_41[ids[:, 41]], tbl_42[ids[:, 42]], tbl_43[ids[:, 43]], tbl_44[ids[:, 44]], tbl_45[ids[:, 45]], tbl_46[ids[:, 46]], tbl_47[ids[:, 47]]], axis=1)
    z = _L0_rec_ref(e, L0_rec_W0, L0_rec_b0, L0_rec_W1, L0_rec_b1)
    z = z.reshape(z.shape[0], -1)
    h = jnp.concatenate([z, dense_ctx], axis=1)
    h = jnp.maximum(h @ W_top1 + b_top1, 0.0)
    h = jnp.maximum(h @ W_top2 + b_top2, 0.0)
    y = h @ W_top3
    return y

_drawn_inputs = setup_inputs


def setup_inputs(seed=0):
    import zlib

    import numpy as np

    out = dict(_drawn_inputs(seed))
    spreads = {'b_top1': (0.0, 2.0),
     'b_top2': (0.0, 0.794),
     'L0_rec_b0': (0.0, 0.1),
     'L0_rec_b1': (0.0, 0.309)}
    factors = {'tbl_0': 8.0,
     'tbl_1': 8.0,
     'tbl_2': 8.0,
     'tbl_3': 8.0,
     'tbl_4': 8.0,
     'tbl_5': 8.0,
     'tbl_6': 8.0,
     'tbl_7': 8.0,
     'tbl_8': 8.0,
     'tbl_9': 8.0,
     'tbl_10': 8.0,
     'tbl_11': 8.0,
     'tbl_12': 8.0,
     'tbl_13': 8.0,
     'tbl_14': 8.0,
     'tbl_15': 8.0,
     'tbl_16': 8.0,
     'tbl_17': 8.0,
     'tbl_18': 8.0,
     'tbl_19': 8.0,
     'tbl_20': 8.0,
     'tbl_21': 8.0,
     'tbl_22': 8.0,
     'tbl_23': 8.0,
     'tbl_24': 8.0,
     'tbl_25': 8.0,
     'tbl_26': 8.0,
     'tbl_27': 8.0,
     'tbl_28': 8.0,
     'tbl_29': 8.0,
     'tbl_30': 8.0,
     'tbl_31': 8.0,
     'tbl_32': 8.0,
     'tbl_33': 8.0,
     'tbl_34': 8.0,
     'tbl_35': 8.0,
     'tbl_36': 8.0,
     'tbl_37': 8.0,
     'tbl_38': 8.0,
     'tbl_39': 8.0,
     'tbl_40': 8.0,
     'tbl_41': 8.0,
     'tbl_42': 8.0,
     'tbl_43': 8.0,
     'tbl_44': 8.0,
     'tbl_45': 8.0,
     'tbl_46': 8.0,
     'tbl_47': 8.0,
     'L0_rec_W0': 7.539,
     'L0_rec_W1': 5.056,
     'dense_ctx': 4.996}
    for name, (base, spread) in spreads.items():
        noise = np.random.default_rng([zlib.crc32(name.encode()), seed]).standard_normal(out[name].shape)
        drawn = base * np.exp(spread * noise) if base else spread * noise
        out[name] = jnp.asarray(drawn.astype(out[name].dtype))
    for name, factor in factors.items():
        out[name] = (out[name] * factor).astype(out[name].dtype)
    return out
```

```python
from collections import namedtuple
from contextlib import ExitStack

import numpy as np

import concourse.bass as bass
from concourse import mybir

F32 = mybir.dt.float32
F32R = mybir.dt.float32r
I32 = mybir.dt.int32
ALU = mybir.AluOpType
ACT = mybir.ActivationFunctionType
AX_X = mybir.AxisListType.X

NF, K, BATCH = 48, 32, 512
C0, HID = 128, 64
N = 512
TB = N // K
TILES = BATCH // TB
NB = 6
NG = 16
NJ1 = HID // NG
FPG = 128 // TB
GATHERS = NF // FPG
XLO = 64
XROWS = XLO + NF
N1, N2, ND = 512, 256, 16
M1, M2 = N1 // 128, N2 // 128

COVER = [
    [[4, 5, 6, 7, 8, 9, 10, 11, 16, 17, 34, 35, 40, 41, 46, 47], [0, 1, 2, 3, 22, 23, 24, 25, 26, 27, 28, 29, 36, 37, 38, 39]],
    [[10, 11, 12, 13, 14, 15, 16, 17, 18, 19, 20, 21, 22, 23, 32, 38], [6, 7, 8, 9, 28, 29, 30, 31, 33, 34, 35, 36, 37, 39, 40, 41]],
    [[16, 17, 28, 29, 30, 31, 32, 33, 34, 35, 42, 43, 44, 45, 46, 47], [0, 1, 2, 3, 4, 5, 12, 13, 14, 15, 18, 19, 20, 21, 22, 23]],
    [[4, 5, 16, 17, 18, 19, 22, 23, 28, 29, 36, 37, 38, 39, 40, 41], [0, 1, 2, 3, 20, 21, 24, 25, 26, 27, 42, 43, 44, 45, 46, 47]],
    [[2, 4, 5, 10, 11, 12, 23, 25, 28, 29, 30, 31, 32, 33, 34, 35], [0, 6, 7, 8, 9, 13, 14, 15, 16, 17, 22, 24, 26, 27, 40, 41]],
    [[10, 11, 18, 19, 20, 21, 22, 23, 34, 35, 42, 43, 44, 45, 46, 47], [0, 1, 2, 3, 4, 5, 12, 14, 17, 30, 31, 32, 33, 38, 40, 41]],
    [[10, 11, 12, 13, 14, 15, 16, 17, 28, 29, 34, 35, 40, 41, 46, 47], [4, 5, 24, 25, 26, 27, 30, 31, 32, 33, 36, 37, 38, 39, 42, 43]],
    [[6, 7, 8, 9, 10, 11, 22, 23, 24, 25, 26, 27, 28, 29, 46, 47], [0, 1, 2, 3, 4, 5, 36, 37, 38, 39, 40, 41, 42, 43, 44, 45]],
]
NI0 = (NB, 4)
CH0, CH1 = sum(NI0), NB * NJ1

Group = namedtuple("Group", "layer j D P F")
GROUPS = [
    Group(1, 0, 1, 3, 2), Group(1, 1, 1, 3, 2), Group(0, 0, 1, 3, 2),
    Group(0, 1, 1, 2, 1), Group(1, 2, 1, 3, 2), Group(1, 3, 1, 3, 2),
]
START = [2, 3]
WHOLE = list(range(len(GROUPS)))
LAST = [0, 1, 4, 5]
MOST_D = max(g.D for g in GROUPS)
MOST_P = max(g.P for g in GROUPS)
MOST_F = max(g.F for g in GROUPS)
assert MOST_D == 1

TAKES = [[[0, 1], [2]], [[3, 4], [5]]]
MAKES = [2, 0, 0, 1, 1, 1, 1]

Step = namedtuple("Step", "q par pos g tile d_before p_before p_freed")


def start_steps():
    out, d, p = [], 0, 0
    for q, pos in enumerate(START):
        g = GROUPS[pos]
        out.append(Step(q, q % 2, pos, g, 0, d, p, None))
        d, p = d + g.D, p + g.P
    return out


def period_steps(n, odd, order):
    d = sum(GROUPS[pos].D for pos in START)
    p = sum(GROUPS[pos].P for pos in START)
    before = GROUPS[START[-1]] if isinstance(n, int) and n == 0 else GROUPS[-1]
    out = []
    for k, pos in enumerate(order):
        g = GROUPS[pos]
        p_before = n * sum(x.P for x in GROUPS) + p
        out.append(Step(n * len(GROUPS) + (len(START) + k), k % 2, pos, g, odd if g.layer else 1 - odd,
                        n * sum(x.D for x in GROUPS) + d, p_before, p_before - before.P))
        d, p, before = d + g.D, p + g.P, g
    return out


def order_of(n):
    return LAST if isinstance(n, int) and n == TILES - 1 else WHOLE


def some(v):
    return not isinstance(v, int) or v > 0


def pair_lanes():
    rows = np.full((2, CH0, 128), -1)
    done = set()
    for j in range(2):
        for i in range(NI0[j]):
            for big_f in range(len(COVER)):
                for lane, g in enumerate(COVER[big_f][j]):
                    f = NB * big_f + i
                    if (min(f, g), max(f, g)) in done:
                        continue
                    done.add((min(f, g), max(f, g)))
                    rows[0, NB * j + i, NG * big_f + lane] = f * NF + g
                    if f != g:
                        rows[1, NB * j + i, NG * big_f + lane] = g * NF + f
    assert len(done) == NF * (NF + 1) // 2
    return rows


def selections():
    b = np.zeros((128, NB, 128), np.float32)
    a0 = np.zeros((128, 2, 128), np.float32)
    a1 = np.zeros((128, NJ1, 128), np.float32)
    for lane in range(128):
        big_f, big_g = divmod(lane, NG)
        for i in range(NB):
            b[[NB * big_f + i, XLO + NB * big_f + i], i, lane] = 1
        for j in range(2):
            g = COVER[big_f][j][big_g]
            a0[[g, XLO + g], j, lane] = 1
        for j in range(NJ1):
            a1[[NJ1 * big_g + j, HID + NJ1 * big_g + j], j, lane] = 1
    return np.concatenate([b, a0, a1], axis=1).reshape(128, -1)


SEL_B, SEL_A0, SEL_A1 = 0, NB, NB + 2
NSEL = NB + 2 + NJ1


def tower_kernel(nc, tables, ids, id_base, select, w0_fg, w0_gf, w1, bias, dense_t, wt1, bt1, wt2, bt2, wt3, y):
    with ExitStack() as ctx:
        def sb(name, shape, dt):
            return ctx.enter_context(nc.sbuf_tensor(name, shape, dt))

        def bank(name):
            return ctx.enter_context(nc.psum_tensor(name, [128, N], F32))

        def sem(name):
            return ctx.enter_context(nc.semaphore(name))

        ids_all = sb("ids_all", [128, TILES * GATHERS], I32)
        base_all = sb("base_all", [128, TILES * GATHERS], I32)
        rows_all = sb("rows_all", [128, TILES * GATHERS], I32)
        row_now = sb("row_now", [128, 2, GATHERS], I32)
        gathered = sb("gathered", [128, 2, GATHERS * K], F32)
        x0 = sb("x0", [NF, 2, N], F32)
        x_stack = sb("x_stack", [128, 2, N], F32R)
        k_stack = sb("k_stack", [128, N], F32R)
        sel = sb("sel", [128, NSEL, 128], F32R)
        B = sb("B", [128, 2, NB, N], F32)
        c_p = sb("c_p", [128, 2, MOST_P, N], F32)
        c_f = sb("c_f", [128, 2, MOST_F, N], F32)
        hi_p = sb("hi_p", [128, 2, MOST_P, N], F32R)
        lo_p = sb("lo_p", [128, 2, MOST_P, N], F32R)
        hi_d = sb("hi_d", [128, 2, MOST_D, N], F32R)
        lo_d = sb("lo_d", [128, 2, MOST_D, N], F32R)
        w_full = [sb("w0_full", [128, CH0, C0], F32), sb("w1_full", [128, CH1, C0], F32)]
        w_hi = [sb("w0_hi", [128, CH0, C0], F32R), sb("w1_hi", [128, CH1, C0], F32R)]
        w_lo = [sb("w0_lo", [128, CH0, C0], F32R), sb("w1_lo", [128, CH1, C0], F32R)]
        biases = sb("biases", [128, 2 + M1 + M2], F32)
        r0 = sb("r0", [128, N], F32)
        r1 = sb("r1", [128, N], F32)
        s0 = sb("s0", [128, BATCH], F32)
        s1 = sb("s1", [128, BATCH], F32)
        wt1_sb = sb("wt1_sb", [128, 2, N1], F32)
        wt2_sb = sb("wt2_sb", [128, M1, N2], F32)
        wt3_sb = sb("wt3_sb", [128, M2], F32)
        y_sb = sb("y_sb", [1, BATCH], F32)
        flat_p = c_p[:].rearrange("p a c n -> p (a c n)")
        sel_raw = flat_p[:, 0:NSEL * 128].rearrange("p (s l) -> p s l", s=NSEL)
        gf_raw = flat_p[:, NSEL * 128:NSEL * 128 + CH0 * C0].rearrange("p (s l) -> p s l", s=CH0)
        h1 = flat_p[:, 0:M1 * N].rearrange("p (m n) -> p m n", m=M1)
        h2 = c_f[:].rearrange("p a c n -> p (a c) n")[:, 0:M2, :]

        z0 = bank("z0")
        z1 = [bank("z1_even"), bank("z1_odd")]
        A = [bank("A_even"), bank("A_odd")]
        B_psum = [bank("B_psum_even"), bank("B_psum_odd")]
        c_d = bank("c_d")

        ids_in = sem("ids_in")
        base_in = sem("base_in")
        sel_in = sem("sel_in")
        w0_fg_in = sem("w0_fg_in")
        w0_gf_in = sem("w0_gf_in")
        w1_in = sem("w1_in")
        bias_in = sem("bias_in")
        mlp_in = sem("mlp_in")
        dense_in = sem("dense_in")
        rows_ready = sem("rows_ready")
        row_now_ready = sem("row_now_ready")
        gather_done = [sem("gather_done_even"), sem("gather_done_odd")]
        x0_in = [sem("x0_in_even"), sem("x0_in_odd")]
        zeroed = sem("zeroed")
        sel_ready = sem("sel_ready")
        w0_summed = sem("w0_summed")
        w_hi_ready = sem("w_hi_ready")
        w_lo_ready = sem("w_lo_ready")
        x_hi = sem("x_hi")
        x_lo = sem("x_lo")
        B_rep = sem("B_rep")
        B_ready = sem("B_ready")
        A_ready = sem("A_ready")
        prod_d = sem("prod_d")
        prod_p = sem("prod_p")
        prod_f = sem("prod_f")
        hi_d_ready = sem("hi_d_ready")
        hi_p_ready = sem("hi_p_ready")
        lo_d_ready = sem("lo_d_ready")
        lo_p_ready = sem("lo_p_ready")
        used_f = sem("used_f")
        used_d = sem("used_d")
        used_p = sem("used_p")
        relu0 = sem("relu0")
        relu1 = sem("relu1")
        k_lo = sem("k_lo")
        sum0 = sem("sum0")
        sum1 = sem("sum1")
        h1_psum = sem("h1_psum")
        h1_ready = sem("h1_ready")
        h2_psum = sem("h2_psum")
        h2_ready = sem("h2_ready")
        y_psum = sem("y_psum")
        y_ready = sem("y_ready")
        y_out = sem("y_out")

        block = ctx.enter_context(nc.Block())

        def all_periods(eng, period):
            period(0, 0)
            period(0, 1)
            with eng.Fori(1, TILES // 2 - 2) as i:
                period(i, 0)
                period(i, 1)
            for i in (TILES // 2 - 2, TILES // 2 - 1):
                period(i, 0)
                period(i, 1)

        def is_at_least(i, odd, n):
            return isinstance(i, int) and 2 * i + odd >= n

        @block.sync
        def _(sp):
            sp.dma_start(ids_all[:], ids).then_inc(ids_in, 16)
            sp.dma_start(base_all[:], id_base).then_inc(base_in, 16)
            sp.dma_start(sel_raw, select.rearrange("p (s l) -> p s l", s=NSEL)).then_inc(sel_in, 16)
            sp.dma_start(w_full[0][:], w0_fg).then_inc(w0_fg_in, 16)
            sp.dma_start(gf_raw, w0_gf).then_inc(w0_gf_in, 16)
            sp.dma_start(biases[:, 0:2], bias).then_inc(bias_in, 16)
            sp.dma_start(w_full[1][:], w1).then_inc(w1_in, 16)

            def place(t_half, odd):
                sp.wait_ge(gather_done[odd], 16 * GATHERS * (t_half + 1))
                if some(2 * t_half + odd - 1):
                    sp.wait_ge(x_lo, 2 * t_half + odd - 1)
                for j in range(GATHERS):
                    sp.dma_start(x0[j * FPG:(j + 1) * FPG, odd, :].rearrange("f (b k) -> f b k", k=K),
                                 gathered[:, odd, j * K:(j + 1) * K]).then_inc(x0_in[odd], 16)

            place(0, 0)
            place(0, 1)
            sp.wait_ge(zeroed, 2)
            sp.dma_start(s0[0:ND, :], dense_t).then_inc(dense_in, 16)
            sp.dma_start(biases[:, 2:2 + M1], bt1).then_inc(mlp_in, 16)
            sp.dma_start(biases[:, 2 + M1:2 + M1 + M2], bt2).then_inc(mlp_in, 16)
            sp.dma_start(wt1_sb[:], wt1.rearrange("(c p) n -> p c n", p=128)).then_inc(mlp_in, 16)
            sp.dma_start(wt2_sb[:], wt2.rearrange("(c p) n -> p c n", p=128)).then_inc(mlp_in, 16)
            sp.dma_start(wt3_sb[:], wt3).then_inc(mlp_in, 16)
            place(1, 0)

            def period(i, odd):
                if not is_at_least(i, odd, TILES - 3):
                    place(i + (3 + odd) // 2, 1 - odd)

            all_periods(sp, period)
            sp.wait_ge(y_ready, 1)
            sp.dma_start(y, y_sb[:]).then_inc(y_out, 16)
            sp.wait_ge(y_out, 16)

        @block.gpsimd
        def _(pool):
            pool.wait_ge(ids_in, 16)
            pool.wait_ge(base_in, 16)
            pool.tensor_tensor(rows_all[:], ids_all[:], base_all[:], ALU.add).then_inc(rows_ready, 1)
            pool.wait_ge(rows_ready, 1)

            def pick_rows(t_half, odd, t):
                if some(t_half):
                    pool.wait_ge(x0_in[odd], 16 * GATHERS * t_half)
                pool.tensor_copy(row_now[:, odd, :], rows_all[:, bass.ds(t * GATHERS, GATHERS)]).then_inc(row_now_ready, 1)
                pool.wait_ge(row_now_ready, t + 1)

            def gather(odd, j):
                pool.indirect_dma_start(gathered[:, odd, j * K:(j + 1) * K], None, tables,
                                        bass.IndirectOffsetOnAxis(row_now[:, odd, j:j + 1], 0)).then_inc(gather_done[odd], 16)

            def lo_parts(s):
                pool.wait_ge(hi_p_ready, s.q + 1)
                if some(s.q - 1):
                    pool.wait_ge(used_p, s.q - 1)
                for c in range(s.g.P):
                    pool.tensor_tensor(lo_p[:, s.par, c, :], c_p[:, s.par, c, :], hi_p[:, s.par, c, :].bitcast(F32),
                                       ALU.subtract).then_inc(lo_p_ready, 1)

            for t in range(2):
                pick_rows(0, t, t)
                for j in range(GATHERS):
                    gather(t, j)
            for s in start_steps():
                lo_parts(s)
            pick_rows(1, 0, 2)
            for j in range(GATHERS):
                gather(0, j)

            def period(i, odd):
                fetch = not is_at_least(i, odd, TILES - 3)
                if fetch:
                    pick_rows(i + (3 + odd) // 2, 1 - odd, 2 * i + (odd + 3))
                for k, s in enumerate(period_steps(2 * i + odd, odd, order_of(2 * i + odd))):
                    lo_parts(s)
                    if fetch:
                        gather(1 - odd, k)

            all_periods(pool, period)

        @block.scalar
        def _(act):
            act.wait_ge(sel_in, 16)
            act.activation(sel[:], sel_raw, ACT.Copy).then_inc(sel_ready, 1)

            def split_x(t_half, odd):
                act.wait_ge(x0_in[odd], 16 * GATHERS * (t_half + 1))
                if some(t_half):
                    q = (2 * (t_half - 1) + (odd - 1)) * len(GROUPS) + len(START) + START[-1]
                    if isinstance(t_half, int) and 2 * t_half + odd == 2:
                        q = 1
                    act.wait_ge(A_ready, q + 1)
                act.activation(x_stack[0:NF, odd, :], x0[:, odd, :], ACT.Copy).then_inc(x_hi, 1)

            def take_B(t, par, i, freed):
                act.wait_ge(B_rep, t * NB + (i + 1))
                if freed is not None:
                    act.wait_ge(freed[0], freed[1])
                act.activation(B[:, par, i, :], B_psum[i % 2][:], ACT.Copy).then_inc(B_ready, 1)

            def hi_part_d(s):
                for d in range(s.g.D):
                    act.wait_ge(prod_d, s.d_before + d + 1)
                    if some(s.q - 1):
                        act.wait_ge(used_d, s.q - 1)
                    act.activation(hi_d[:, s.par, d, :], c_d[:], ACT.Copy).then_inc(hi_d_ready, 1)

            def hi_parts_p(s):
                act.wait_ge(prod_p, s.q + 1)
                if some(s.q - 1):
                    act.wait_ge(used_p, s.q - 1)
                act.activation(hi_p[:, s.par, 0:s.g.P, :], c_p[:, s.par, 0:s.g.P, :], ACT.Copy).then_inc(hi_p_ready, 1)

            def relu_0(t, q_last, q_copied):
                act.wait_ge(used_p, q_last + 1)
                if q_copied is not None:
                    act.wait_ge(A_ready, q_copied + 1)
                    act.wait_ge(sum0, t)
                act.activation(k_stack[0:HID, :], z0[0:HID, :], ACT.Relu, bias=biases[0:HID, 0:1])
                act.activation(r0[:], z0[:], ACT.Relu, bias=biases[:, 0:1]).then_inc(relu0, 1)

            def relu_1(n, odd, q_last):
                act.wait_ge(used_p, q_last + 1)
                if some(n):
                    act.wait_ge(sum1, n)
                act.activation(r1[:], z1[odd][:], ACT.Relu, bias=biases[:, 1:2]).then_inc(relu1, 1)

            act.wait_ge(zeroed, 2)
            split_x(0, 0)
            act.wait_ge(w0_summed, 1)
            act.activation(w_hi[0][:], w_full[0][:], ACT.Copy).then_inc(w_hi_ready, 1)
            for i in range(NB):
                take_B(0, 0, i, None)
            split_x(0, 1)
            act.wait_ge(w1_in, 16)
            act.activation(w_hi[1][:], w_full[1][:], ACT.Copy).then_inc(w_hi_ready, 1)
            for s in start_steps():
                hi_part_d(s)
                hi_parts_p(s)
            act.wait_ge(bias_in, 16)
            relu_0(0, len(START) - 1, None)

            def period(i, odd):
                n = 2 * i + odd
                last = is_at_least(i, odd, TILES - 1)
                steps = period_steps(n, odd, order_of(n))
                first = not some(n)

                def next_B(lot):
                    for b in lot:
                        freed = None
                        if not first:
                            g = GROUPS[-1]
                            if b < g.D:
                                freed = (prod_d, steps[0].d_before - g.D + b + 1)
                            else:
                                freed = (prod_p if b < g.D + g.P else prod_f, steps[0].q)
                        take_B(n + 1, 1 - odd, b, freed)

                for k, s in enumerate(steps):
                    hi_part_d(s)
                    if k <= 1 and not last:
                        next_B(TAKES[k][0])
                    if s.pos == 5 and not last:
                        relu_0(n + 1, steps[3].q, steps[5].q)
                    hi_parts_p(s)
                    if k <= 1 and not last:
                        next_B(TAKES[k][1])
                    if k == 2 and not first:
                        relu_1(n - 1, 1 - odd, steps[0].q - 1)
                    if s.pos == 2 and not is_at_least(i, odd, TILES - 2):
                        split_x(i + 1, odd)

            all_periods(act, period)
            end = period_steps(TILES - 1, 1, LAST)
            relu_1(TILES - 1, 1, end[-1].q)
            act.wait_ge(mlp_in, 16 * 5)
            for m in range(M1):
                act.wait_ge(h1_psum, m + 1)
                act.activation(h1[:, m, :], [A[0], A[1], *B_psum][m][:], ACT.Relu,
                               bias=biases[:, 2 + m:3 + m]).then_inc(h1_ready, 1)
            for m in range(M2):
                act.wait_ge(h2_psum, m + 1)
                act.activation(h2[:, m, :], [z0, c_d][m][:], ACT.Relu,
                               bias=biases[:, 2 + M1 + m:3 + M1 + m]).then_inc(h2_ready, 1)
            act.wait_ge(y_psum, 1)
            act.activation(y_sb[:], z1[0][0:1, :], ACT.Copy).then_inc(y_ready, 1)

        @block.vector
        def _(dve):
            dve.memset(x_stack[:].bitcast(F32), 0.0).then_inc(zeroed, 1)
            dve.memset(s0[0:HID, :], 0.0).then_inc(zeroed, 1)

            def split_x(t, odd):
                dve.wait_ge(x_hi, t + 1)
                dve.tensor_tensor(x_stack[XLO:XROWS, odd, :], x0[:, odd, :], x_stack[0:NF, odd, :].bitcast(F32),
                                  ALU.subtract).then_inc(x_lo, 1)

            def products(s):
                dve.wait_ge(A_ready, s.q + 1)
                a = A[s.par][:]
                for d in range(s.g.D):
                    if some(s.d_before + d):
                        dve.wait_ge(lo_d_ready, s.d_before + d)
                    dve.tensor_tensor(c_d[:], B[:, s.tile, d, :], a, ALU.mult).then_inc(prod_d, 1)
                wide = a.rearrange("p (o n) -> p o n", o=1)
                if s.p_freed is not None:
                    dve.wait_ge(lo_p_ready, s.p_freed)
                dve.tensor_tensor(c_p[:, s.par, 0:s.g.P, :], B[:, s.tile, s.g.D:s.g.D + s.g.P, :],
                                  wide.to_broadcast([128, s.g.P, N]), ALU.mult).then_inc(prod_p, 1)
                if some(s.q - 1):
                    dve.wait_ge(used_f, s.q - 1)
                first_f = s.g.D + s.g.P
                dve.tensor_tensor(c_f[:, s.par, 0:s.g.F, :], B[:, s.tile, first_f:first_f + s.g.F, :],
                                  wide.to_broadcast([128, s.g.F, N]), ALU.mult).then_inc(prod_f, 1)
                for d in range(s.g.D):
                    dve.wait_ge(hi_d_ready, s.d_before + d + 1)
                    if some(s.q - 1):
                        dve.wait_ge(used_d, s.q - 1)
                    dve.tensor_tensor(lo_d[:, s.par, d, :], c_d[:], hi_d[:, s.par, d, :].bitcast(F32),
                                      ALU.subtract).then_inc(lo_d_ready, 1)

            def split_k_and_sum_0(t, column):
                dve.wait_ge(relu0, t + 1)
                dve.tensor_tensor(k_stack[HID:, :], r0[0:HID, :], k_stack[0:HID, :].bitcast(F32),
                                  ALU.subtract).then_inc(k_lo, 1)
                dve.tensor_reduce(s0[HID:, bass.ds(column, TB)], r0[HID:, :].rearrange("p (b k) -> p b k", k=K),
                                  AX_X, ALU.add).then_inc(sum0, 1)

            def sum_1(n, column):
                dve.wait_ge(relu1, n + 1)
                dve.tensor_reduce(s1[:, bass.ds(column, TB)], r1[:].rearrange("p (b k) -> p b k", k=K),
                                  AX_X, ALU.add).then_inc(sum1, 1)

            split_x(0, 0)
            dve.wait_ge(w0_fg_in, 16)
            dve.wait_ge(w0_gf_in, 16)
            dve.tensor_tensor(w_full[0][:], w_full[0][:], gf_raw, ALU.add).then_inc(w0_summed, 1)
            dve.wait_ge(w0_summed, 1)
            dve.wait_ge(w_hi_ready, 1)
            dve.tensor_tensor(w_lo[0][:], w_full[0][:], w_hi[0][:].bitcast(F32), ALU.subtract).then_inc(w_lo_ready, 1)
            dve.wait_ge(sel_ready, 1)
            dve.wait_ge(B_ready, NB)
            first, second = start_steps()
            products(first)
            split_x(1, 1)
            products(second)
            dve.wait_ge(w_hi_ready, 2)
            dve.tensor_tensor(w_lo[1][:], w_full[1][:], w_hi[1][:].bitcast(F32), ALU.subtract).then_inc(w_lo_ready, 1)
            split_k_and_sum_0(0, 0)

            def period(i, odd):
                n = 2 * i + odd
                for k, s in enumerate(period_steps(n, odd, order_of(n))):
                    if s.pos == 2:
                        dve.wait_ge(B_ready, NB * (n + 2))
                    products(s)
                    if k == 3 and some(n):
                        sum_1(n - 1, (n - 1) * TB)
                    if s.pos == 3 and not is_at_least(i, odd, TILES - 2):
                        split_x(n + 2, odd)
                    if s.pos == 5 and not is_at_least(i, odd, TILES - 1):
                        split_k_and_sum_0(n + 1, (n + 1) * TB)

            all_periods(dve, period)
            sum_1(TILES - 1, (TILES - 1) * TB)

        @block.tensor
        def _(pe):
            def copy_B(t, par, i):
                if some(t * NB + (i - 1)):
                    pe.wait_ge(B_ready, t * NB + (i - 1))
                pe.matmul(B_psum[i % 2][:], sel[0:XROWS, SEL_B + i, :], x_stack[0:XROWS, par, :],
                          start=True, stop=True).then_inc(B_rep, 1)

            def copy_A(s, t):
                if some(s.q - 1):
                    pe.wait_ge(prod_f, s.q - 1)
                if s.g.layer == 0:
                    pe.wait_ge(x_lo, t + 1)
                    pe.matmul(A[s.par][:], sel[0:XROWS, SEL_A0 + s.g.j, :], x_stack[0:XROWS, s.tile, :],
                              start=True, stop=True).then_inc(A_ready, 1)
                else:
                    pe.wait_ge(k_lo, t + 1)
                    pe.matmul(A[s.par][:], sel[:, SEL_A1 + s.g.j, :], k_stack[:],
                              start=True, stop=True).then_inc(A_ready, 1)

            def chunks(s, between=None):
                layer, g = s.g.layer, s.g
                z = z1[s.tile] if layer else z0
                opens = g.j == 0
                closes = g.j == (NJ1 - 1 if layer else 1)
                for f in range(g.F):
                    i = g.D + g.P + f
                    if f == 0:
                        pe.wait_ge(prod_f, s.q + 1)
                    last = pe.matmul(z[:], w_full[layer][:, NB * g.j + i, :], c_f[:, s.par, f, :],
                                     start=opens and f == 0, stop=False)
                    if f == g.F - 1:
                        last.then_inc(used_f, 1)
                    if between:
                        between()
                for kind, count, hi, lo, before, ready, used in (
                        ("D", g.D, hi_d, lo_d, s.d_before, lo_d_ready, used_d),
                        ("P", g.P, hi_p, lo_p, s.p_before, lo_p_ready, used_p)):
                    for c in range(count):
                        i = c + (g.D if kind == "P" else 0)
                        pe.wait_ge(ready, before + c + 1)
                        w = NB * g.j + i
                        pe.matmul(z[:], w_hi[layer][:, w, :], hi[:, s.par, c, :], start=False, stop=False)
                        pe.matmul(z[:], w_hi[layer][:, w, :], lo[:, s.par, c, :], start=False, stop=False)
                        ends = c == count - 1
                        last = pe.matmul(z[:], w_lo[layer][:, w, :], hi[:, s.par, c, :], start=False,
                                         stop=closes and kind == "P" and ends)
                        if ends:
                            last.then_inc(used, 1)
                        if between:
                            between()

            pe.wait_ge(sel_ready, 1)
            pe.wait_ge(x_lo, 1)
            for i in range(NB):
                copy_B(0, 0, i)
            first, second = start_steps()
            copy_A(first, 0)
            copy_A(second, 0)
            pe.wait_ge(w_lo_ready, 1)
            chunks(first)
            chunks(second)
            ahead = period_steps(0, 0, WHOLE)
            copy_A(ahead[0], 0)
            copy_A(ahead[1], 0)
            for i in range(NB):
                if i == 0:
                    pe.wait_ge(x_lo, 2)
                copy_B(1, 1, i)
            pe.wait_ge(w_lo_ready, 2)

            def period(i, odd):
                n = 2 * i + odd
                steps = period_steps(n, odd, order_of(n))
                ahead = []
                if not is_at_least(i, odd, TILES - 1):
                    ahead = period_steps(n + 1, 1 - odd, order_of(n + 1))[:2]
                targets = [(s, n if s.g.layer else n + 1) for s in steps[2:]]
                targets += [(s, n + 1) for s in ahead]
                for k, s in enumerate(steps):
                    if k < len(targets) and s.pos != 4:
                        copy_A(*targets[k])
                    if s.pos == 0 and some(n - 1):
                        pe.wait_ge(relu1, n - 1)
                    if s.pos == 2:
                        pe.wait_ge(relu0, n + 1)
                    if s.pos == 5 and not is_at_least(i, odd, TILES - 2):
                        pe.wait_ge(x_lo, n + 3)
                        left = iter(range(NB))
                        lots = iter(MAKES)

                        def some_B():
                            for _ in range(next(lots)):
                                copy_B(n + 2, odd, next(left))

                        some_B()
                        chunks(s, some_B)
                    else:
                        chunks(s)
                    if k < len(targets) and s.pos == 4:
                        copy_A(*targets[k])

            all_periods(pe, period)

            pe.wait_ge(sum0, TILES)
            pe.wait_ge(sum1, TILES)
            pe.wait_ge(dense_in, 16)
            pe.wait_ge(mlp_in, 16 * 5)
            for m in range(M1):
                out = [A[0], A[1], *B_psum][m]
                pe.matmul(out[:], wt1_sb[:, 0, m * 128:(m + 1) * 128], s0[:], start=True, stop=False)
                pe.matmul(out[:], wt1_sb[:, 1, m * 128:(m + 1) * 128], s1[:], start=False, stop=True).then_inc(h1_psum, 1)
            for m in range(M2):
                for c in range(M1):
                    if m == 0:
                        pe.wait_ge(h1_ready, c + 1)
                    last = pe.matmul([z0, c_d][m][:], wt2_sb[:, c, m * 128:(m + 1) * 128], h1[:, c, :],
                                     start=c == 0, stop=c == M1 - 1)
                last.then_inc(h2_psum, 1)
            for m in range(M2):
                pe.wait_ge(h2_ready, m + 1)
                last = pe.matmul(z1[0][0:1, :], wt3_sb[:, m:m + 1], h2[:, m, :], start=m == 0, stop=m == M2 - 1)
            last.then_inc(y_psum, 1)


def kernel(**inputs):
    import concourse.bacc as _bacc
    from concourse.bass_utils import run_bass_kernel_spmd as _run

    tables = [np.asarray(inputs[f"tbl_{f}"]) for f in range(NF)]
    sizes = [t.shape[0] for t in tables]
    starts = np.concatenate([[0], np.cumsum(sizes)[:-1]]).astype(np.int32)

    def by_lane(a):
        a = a.reshape(TILES, TB, GATHERS, FPG)
        return np.ascontiguousarray(a.transpose(3, 1, 0, 2).reshape(128, TILES * GATHERS))

    fg, gf = pair_lanes()
    w0 = np.asarray(inputs["L0_rec_W0"])
    w0 = np.concatenate([w0, np.zeros((1, C0), w0.dtype)])
    w1 = np.asarray(inputs["L0_rec_W1"]).reshape(128 // NG, NB, NG, NJ1, C0)
    wt1 = np.asarray(inputs["W_top1"])
    nz = HID + C0
    arrays = {
        "tables": np.concatenate(tables),
        "ids": by_lane(np.asarray(inputs["ids"])),
        "id_base": by_lane(np.broadcast_to(starts, (BATCH, NF))),
        "select": selections(),
        "w0_fg": w0[fg.T],
        "w0_gf": w0[gf.T],
        "w1": w1.transpose(0, 2, 3, 1, 4).reshape(128, CH1, C0),
        "bias": np.stack([np.asarray(inputs["L0_rec_b0"]), np.asarray(inputs["L0_rec_b1"])], axis=1),
        "dense_t": np.asarray(inputs["dense_ctx"]).T,
        "wt1": np.concatenate([wt1[nz:], np.zeros((HID - ND, N1), wt1.dtype), wt1[:HID], wt1[HID:nz]]),
        "bt1": np.asarray(inputs["b_top1"]).reshape(M1, 128).T,
        "wt2": np.asarray(inputs["W_top2"]),
        "bt2": np.asarray(inputs["b_top2"]).reshape(M2, 128).T,
        "wt3": np.asarray(inputs["W_top3"]).reshape(M2, 128).T,
    }
    nc = _bacc.Bacc("TRN2", target_bir_lowering=False, num_devices=1)
    args = []
    for name, a in arrays.items():
        arrays[name] = a = np.ascontiguousarray(a)
        args.append(nc.dram_tensor(name, a.shape, mybir.dt.from_np(a.dtype), kind="ExternalInput").ap())
    args.append(nc.dram_tensor("y", (BATCH, 1), F32, kind="ExternalOutput").ap().rearrange("b o -> o b"))
    tower_kernel(nc, *args)
    r = _run(nc, [arrays], core_ids=[0])
    return r.results[0]["y"]
```

```python
from collections import namedtuple
from contextlib import ExitStack

import numpy as np

import concourse.bass as bass
from concourse import mybir

F32 = mybir.dt.float32
F32R = mybir.dt.float32r
F16 = mybir.dt.float16
I32 = mybir.dt.int32
ALU = mybir.AluOpType
ACT = mybir.ActivationFunctionType
AX_X = mybir.AxisListType.X

NF, K, BATCH = 48, 32, 512
C0, HID = 128, 64
N = 512
TB = N // K
TILES = BATCH // TB
NB = 6
NG = 16
NJ1 = HID // NG
FPG = 128 // TB
GATHERS = NF // FPG
XLO = 64
XROWS = XLO + NF
N1, N2, ND = 512, 256, 16
M1, M2 = N1 // 128, N2 // 128

COVER = [
    [[4, 5, 6, 7, 8, 9, 10, 11, 16, 17, 34, 35, 40, 41, 46, 47],
     [0, 1, 2, 3, 22, 23, 24, 25, 26, 27, 28, 29, 36, 37, 38, 39]],
    [[10, 11, 12, 13, 14, 15, 16, 17, 18, 19, 20, 21, 22, 23, 32, 38],
     [6, 7, 8, 9, 28, 29, 30, 31, 33, 34, 35, 36, 37, 39, 40, 41]],
    [[16, 17, 28, 29, 30, 31, 32, 33, 34, 35, 42, 43, 44, 45, 46, 47],
     [0, 1, 2, 3, 4, 5, 12, 13, 14, 15, 18, 19, 20, 21, 22, 23]],
    [[4, 5, 16, 17, 18, 19, 22, 23, 28, 29, 36, 37, 38, 39, 40, 41],
     [0, 1, 2, 3, 20, 21, 24, 25, 26, 27, 42, 43, 44, 45, 46, 47]],
    [[2, 4, 5, 10, 11, 12, 23, 25, 28, 29, 30, 31, 32, 33, 34, 35],
     [0, 6, 7, 8, 9, 13, 14, 15, 16, 17, 22, 24, 26, 27, 40, 41]],
    [[10, 11, 18, 19, 20, 21, 22, 23, 34, 35, 42, 43, 44, 45, 46, 47],
     [0, 1, 2, 3, 4, 5, 12, 14, 17, 30, 31, 32, 33, 38, 40, 41]],
    [[10, 11, 12, 13, 14, 15, 16, 17, 28, 29, 34, 35, 40, 41, 46, 47],
     [4, 5, 24, 25, 26, 27, 30, 31, 32, 33, 36, 37, 38, 39, 42, 43]],
    [[6, 7, 8, 9, 10, 11, 22, 23, 24, 25, 26, 27, 28, 29, 46, 47],
     [0, 1, 2, 3, 4, 5, 36, 37, 38, 39, 40, 41, 42, 43, 44, 45]],
]
NI0 = (NB, 4)
CH0, CH1 = sum(NI0), NB * NJ1

Group = namedtuple("Group", "layer j D P F")
GROUPS = [
    Group(1, 0, 1, 3, 2), Group(1, 1, 1, 3, 2), Group(0, 0, 1, 2, 3),
    Group(0, 1, 1, 2, 1), Group(1, 2, 1, 3, 2), Group(1, 3, 1, 3, 2),
]
START = [2, 3]
WHOLE = list(range(len(GROUPS)))
FIRST = [2, 3, 0, 1, 4, 5]
LAST = [0, 1, 4, 5]
B_PARTS = [(0, GROUPS[-1].D + GROUPS[-1].P), (GROUPS[-1].D + GROUPS[-1].P, NB)]
assert GROUPS[-1].D == 1
W1_LOTS = [slice(NB * j, NB * (j + 1)) for j in range(NJ1)]
MOST_D = max(g.D for g in GROUPS)
MOST_P = max(g.P for g in GROUPS)
MOST_F = max(g.F for g in GROUPS)

MAKES = {4: 5, 5: 2}
FIRST_MAKES = 3
WARM_UP = 10
LO_LOTS = {2: [2], 3: [1, 2]}

DEPTH = 3

Step = namedtuple("Step", "q par slot pos g tile d_par d_before p_before p_freed")


def start_steps():
    out, d, p = [], 0, 0
    for q, pos in enumerate(START):
        g = GROUPS[pos]
        out.append(Step(q, q % 2, q % DEPTH, pos, g, 0, d % 2, d, p, 0))
        d, p = d + g.D, p + g.P
    return out


def period_steps(n, odd, order):
    d = sum(GROUPS[pos].D for pos in START)
    p = sum(GROUPS[pos].P for pos in START)
    start = isinstance(n, int) and n == 0
    before = [GROUPS[x].P for x in (START if start else WHOLE[1 - DEPTH:])]
    out = []
    for k, pos in enumerate(order):
        g = GROUPS[pos]
        p_before = n * sum(x.P for x in GROUPS) + p
        d_par = (odd * sum(x.D for x in GROUPS) + d) % 2
        out.append(Step(n * len(GROUPS) + (len(START) + k), k % 2, (len(START) + k) % DEPTH, pos, g,
                        odd if g.layer else 1 - odd, d_par,
                        n * sum(x.D for x in GROUPS) + d, p_before, p_before - sum(before[1 - DEPTH:])))
        d, p = d + g.D, p + g.P
        before.append(g.P)
    return out


def order_of(n):
    if isinstance(n, int) and n == 0:
        return FIRST
    return LAST if isinstance(n, int) and n == TILES - 1 else WHOLE


def some(v):
    return not isinstance(v, int) or v > 0


def pair_lanes():
    rows = np.full((2, CH0, 128), -1)
    done = set()
    for j in range(2):
        for i in range(NI0[j]):
            for big_f in range(len(COVER)):
                for lane, g in enumerate(COVER[big_f][j]):
                    f = NB * big_f + i
                    if (min(f, g), max(f, g)) in done:
                        continue
                    done.add((min(f, g), max(f, g)))
                    rows[0, NB * j + i, NG * big_f + lane] = f * NF + g
                    if f != g:
                        rows[1, NB * j + i, NG * big_f + lane] = g * NF + f
    assert len(done) == NF * (NF + 1) // 2
    return rows


def selections():
    a0 = np.zeros((128, 2, 128), np.float32)
    a1 = np.zeros((128, NJ1, 128), np.float32)
    for lane in range(128):
        big_f, big_g = divmod(lane, NG)
        for j in range(2):
            g = COVER[big_f][j][big_g]
            a0[[g, XLO + g], j, lane] = 1
        for j in range(NJ1):
            a1[[NJ1 * big_g + j, HID + NJ1 * big_g + j], j, lane] = 1
    return np.concatenate([a0, a1], axis=1).reshape(128, -1).astype(np.float16)


SEL_A0, SEL_A1 = 0, 2
NSEL = 2 + NJ1


def tower_kernel(nc, tables, ids, id_base, select, w0_fg, w0_gf, w1, bias, dense_t, wt1, bt1, wt2, bt2, wt3, y):
    with ExitStack() as ctx:
        def sb(name, shape, dt):
            return ctx.enter_context(nc.sbuf_tensor(name, shape, dt))

        def bank(name):
            return ctx.enter_context(nc.psum_tensor(name, [128, N], F32))

        def sem(name):
            return ctx.enter_context(nc.semaphore(name))

        ids_all = sb("ids_all", [128, TILES * GATHERS], I32)
        base_all = sb("base_all", [128, TILES * GATHERS], I32)
        rows_all = sb("rows_all", [128, TILES * GATHERS], I32)
        row_now = sb("row_now", [128, 2, GATHERS], I32)
        gathered = sb("gathered", [128, 2, GATHERS * K], F32)
        gathered_parts = sb("gathered_parts", [128, 2, 2, GATHERS * K], F32R)
        x_dram = [nc.dram_tensor(f"x_{i}", (GATHERS, FPG, TB, K), F32, kind="Internal").ap() for i in range(2)]
        parts_dram = [nc.dram_tensor(f"x_parts_{i}", (2, GATHERS, FPG, TB, K), F32, kind="Internal").ap()
                      for i in range(2)]
        x_stack = sb("x_stack", [128, 2, N], F32R)
        k_stack = sb("k_stack", [128, N], F32R)
        sel = sb("sel", [128, NSEL, 128], F32R)
        B = sb("B", [128, 2, NB, N], F32)
        c_p = sb("c_p", [128, DEPTH, MOST_P, N], F32)
        c_f = sb("c_f", [128, DEPTH, MOST_F, N], F32)
        hi_p = sb("hi_p", [128, DEPTH, MOST_P, N], F32R)
        lo_p = sb("lo_p", [128, DEPTH, MOST_P, N], F32R)
        hi_d = sb("hi_d", [128, DEPTH, MOST_D, N], F32R)
        lo_d = sb("lo_d", [128, DEPTH, MOST_D, N], F32R)
        w_full = [sb("w0_full", [128, CH0, C0], F32), sb("w1_full", [128, CH1, C0], F32)]
        w_hi = [sb("w0_hi", [128, CH0, C0], F32R), sb("w1_hi", [128, CH1, C0], F32R)]
        w_lo = [sb("w0_lo", [128, CH0, C0], F32R), sb("w1_lo", [128, CH1, C0], F32R)]
        biases = sb("biases", [128, 2 + M1 + M2], F32)
        r0 = sb("r0", [128, N], F32)
        r1 = sb("r1", [128, N], F32)
        s0 = sb("s0", [128, BATCH], F32)
        s1 = sb("s1", [128, BATCH], F32)
        wt1_sb = sb("wt1_sb", [128, 2, N1], F32)
        wt2_sb = sb("wt2_sb", [128, M1, N2], F32)
        wt3_sb = sb("wt3_sb", [128, M2], F32)
        y_sb = sb("y_sb", [1, BATCH], F32)
        flat_p = c_p[:].rearrange("p a c n -> p (a c n)")
        sel_raw = flat_p[:, 0:NSEL * 64].bitcast(F16).rearrange("p (s l) -> p s l", s=NSEL)
        gf_raw = flat_p[:, NSEL * 128:NSEL * 128 + CH0 * C0].rearrange("p (s l) -> p s l", s=CH0)
        h1 = flat_p[:, 0:M1 * N].rearrange("p (m n) -> p m n", m=M1)
        h2 = c_f[:].rearrange("p a c n -> p (a c) n")[:, 0:M2, :]

        z0 = bank("z0")
        z1 = [bank("z1_even"), bank("z1_odd")]
        A = [bank("A_even"), bank("A_odd")]
        c_d = [bank("c_d_even"), bank("c_d_odd")]
        spare = bank("spare")
        last_par = period_steps(TILES - 1, 1, LAST)[-1].par
        h1_banks = [spare, z0, z1[0], A[1 - last_par]]
        h2_banks = [A[last_par], c_d[0]]

        ids_in = sem("ids_in")
        base_in = sem("base_in")
        sel_in = sem("sel_in")
        w0_fg_in = sem("w0_fg_in")
        w0_gf_in = sem("w0_gf_in")
        w1_in = sem("w1_in")
        bias_in = sem("bias_in")
        mlp_in = sem("mlp_in")
        dense_in = sem("dense_in")
        rows_ready = sem("rows_ready")
        row_now_ready = sem("row_now_ready")
        gather_done = [sem("gather_done_even"), sem("gather_done_odd")]
        x_out = [sem("x_out_even"), sem("x_out_odd")]
        x_in = [sem("x_in_even"), sem("x_in_odd")]
        zeroed = sem("zeroed")
        sel_ready = sem("sel_ready")
        w0_summed = sem("w0_summed")
        w_hi_ready = sem("w_hi_ready")
        w_lo_ready = sem("w_lo_ready")
        x_hi = sem("x_hi")
        x_lo = sem("x_lo")
        x_raw_out = [sem("x_raw_out_even"), sem("x_raw_out_odd")]
        B_in = [[sem(f"B_{part}_in_{par}") for part in ("first", "rest")] for par in ("even", "odd")]
        A_ready = sem("A_ready")
        prod_d = sem("prod_d")
        prod_p = sem("prod_p")
        prod_f = sem("prod_f")
        hi_d_ready = sem("hi_d_ready")
        hi_p_ready = sem("hi_p_ready")
        lo_d_ready = sem("lo_d_ready")
        lo_p_ready = sem("lo_p_ready")
        used_f = sem("used_f")
        used_d = sem("used_d")
        used_p = sem("used_p")
        relu0 = sem("relu0")
        relu1 = sem("relu1")
        k_lo = sem("k_lo")
        sum0 = sem("sum0")
        sum1 = sem("sum1")
        h1_psum = sem("h1_psum")
        h1_ready = sem("h1_ready")
        h2_psum = sem("h2_psum")
        h2_ready = sem("h2_ready")
        y_psum = sem("y_psum")
        y_ready = sem("y_ready")
        y_out = sem("y_out")

        block = ctx.enter_context(nc.Block())

        def all_periods(eng, period):
            period(0, 0)
            period(0, 1)
            with eng.Fori(1, TILES // 2 - 2) as i:
                period(i, 0)
                period(i, 1)
            for i in (TILES // 2 - 2, TILES // 2 - 1):
                period(i, 0)
                period(i, 1)

        def is_at_least(i, odd, n):
            return isinstance(i, int) and 2 * i + odd >= n

        @block.sync
        def _(sp):
            sp.dma_start(ids_all[:], ids).then_inc(ids_in, 16)
            sp.dma_start(base_all[:], id_base).then_inc(base_in, 16)
            sp.dma_start(sel_raw, select.rearrange("p (s l) -> p s l", s=NSEL)).then_inc(sel_in, 16)
            sp.dma_start(w_full[0][:], w0_fg).then_inc(w0_fg_in, 16)
            sp.dma_start(gf_raw, w0_gf).then_inc(w0_gf_in, 16)
            sp.dma_start(biases[:, 0:2], bias).then_inc(bias_in, 16)

            def place(t_half, odd):
                t = 2 * t_half + odd
                copied = 2 * t - 2 if isinstance(t_half, int) and t <= 3 else (
                    (t - 3) * len(GROUPS) + (len(START) + START[-1] + 1))
                if some(t_half):
                    sp.wait_ge(A_ready, copied)
                sp.wait_ge(gather_done[odd], 16 * GATHERS * (t_half + 1))
                sp.dma_start(x_dram[odd].rearrange("j f b k -> (f b) j k"),
                             gathered[:, odd, :].rearrange("p (j k) -> p j k", k=K)).then_inc(x_raw_out[odd], 16)
                sp.wait_ge(x_lo, t + 1)
                sp.dma_start(parts_dram[odd].rearrange("h j f b k -> (f b) (h j) k"),
                             gathered_parts[:, odd, :, :].rearrange("p h (j k) -> p (h j) k", k=K)
                             .bitcast(F32)).then_inc(x_out[odd], 16)
                sp.wait_ge(x_out[odd], 16 * (t_half + 1))
                sp.wait_ge(x_raw_out[odd], 16 * (t_half + 1))
                for part, row in enumerate((0, XLO)):
                    sp.dma_start(x_stack[row:row + NF, odd, :].bitcast(F32),
                                 parts_dram[odd][part].rearrange("j f b k -> (j f) (b k)")).then_inc(x_in[odd], 16)
                if some(t_half + odd):
                    for part in range(2):
                        sp.wait_ge(B_in[1 - odd][part], 16 * (t_half + odd))
                for part, (lo, hi) in enumerate(B_PARTS):
                    if some(t_half):
                        sp.wait_ge((prod_p, prod_f)[part], (t - 2) * len(GROUPS) + (len(START) + len(GROUPS)))
                    sp.dma_start(B[:, odd, lo:hi, :], x_dram[odd].rearrange("j f b k -> (j f) (b k)")
                                 .rearrange("(F o i) n -> F o i n", i=NB, o=1)[:, :, lo:hi, :]
                                 .to_broadcast([NF // NB, NG, hi - lo, N])).then_inc(B_in[odd][part], 16)

            sp.wait_ge(zeroed, 2)
            place(0, 0)
            place(0, 1)
            sp.dma_start(w_full[1][:], w1).then_inc(w1_in, 16)
            sp.dma_start(s0[0:ND, :], dense_t).then_inc(dense_in, 16)
            sp.dma_start(biases[:, 2:2 + M1], bt1).then_inc(mlp_in, 16)
            sp.dma_start(biases[:, 2 + M1:2 + M1 + M2], bt2).then_inc(mlp_in, 16)
            sp.dma_start(wt1_sb[:], wt1.rearrange("(c p) n -> p c n", p=128)).then_inc(mlp_in, 16)
            sp.dma_start(wt2_sb[:], wt2.rearrange("(c p) n -> p c n", p=128)).then_inc(mlp_in, 16)
            sp.dma_start(wt3_sb[:], wt3).then_inc(mlp_in, 16)

            def period(i, odd):
                if not is_at_least(i, odd, TILES - 2):
                    place(i + 1, odd)

            all_periods(sp, period)
            sp.wait_ge(y_ready, 1)
            sp.dma_start(y, y_sb[:]).then_inc(y_out, 16)
            sp.wait_ge(y_out, 16)

        @block.gpsimd
        def _(pool):
            pool.wait_ge(ids_in, 16)
            pool.wait_ge(base_in, 16)
            pool.tensor_tensor(rows_all[:], ids_all[:], base_all[:], ALU.add).then_inc(rows_ready, 1)
            pool.wait_ge(rows_ready, 1)

            def pick_rows(odd, t, raw_out_before):
                if some(t - 1):
                    pool.wait_ge(x_lo, t - 1)
                    pool.wait_ge(x_raw_out[odd], raw_out_before)
                pool.tensor_copy(row_now[:, odd, :],
                                 rows_all[:, bass.ds(t * GATHERS, GATHERS)]).then_inc(row_now_ready, 1)
                pool.wait_ge(row_now_ready, t + 1)

            def gather(odd, j):
                pool.indirect_dma_start(gathered[:, odd, j * K:(j + 1) * K], None, tables,
                                        bass.IndirectOffsetOnAxis(row_now[:, odd, j:j + 1], 0)
                                        ).then_inc(gather_done[odd], 16)

            def lo_parts(s):
                pool.wait_ge(hi_p_ready, s.q + 1)
                if some(s.q - (DEPTH - 1)):
                    pool.wait_ge(used_p, s.q - (DEPTH - 1))
                first = 0
                for count in LO_LOTS[s.g.P]:
                    lot = slice(first, first + count)
                    pool.tensor_tensor(lo_p[:, s.slot, lot, :], c_p[:, s.slot, lot, :],
                                       hi_p[:, s.slot, lot, :].bitcast(F32), ALU.subtract).then_inc(lo_p_ready, count)
                    first += count

            for t in range(3):
                pick_rows(t % 2, t, 16 * (t // 2))
                for j in range(GATHERS):
                    gather(t % 2, j)
            for s in start_steps():
                lo_parts(s)

            def period(i, odd):
                fetch = not is_at_least(i, odd, TILES - 3)
                if fetch:
                    pick_rows(1 - odd, 2 * i + (odd + 3), 16 * (i + 1 + odd))
                for k, s in enumerate(period_steps(2 * i + odd, odd, order_of(2 * i + odd))):
                    lo_parts(s)
                    if fetch:
                        gather(1 - odd, k)

            all_periods(pool, period)

        @block.scalar
        def _(act):
            act.wait_ge(sel_in, 16)
            act.activation(sel[:], sel_raw, ACT.Copy).then_inc(sel_ready, 1)

            def split_x(t_half, odd):
                act.wait_ge(gather_done[odd], 16 * GATHERS * (t_half + 1))
                if some(t_half):
                    act.wait_ge(x_out[odd], 16 * t_half)
                act.activation(gathered_parts[:, odd, 0, :], gathered[:, odd, :], ACT.Copy).then_inc(x_hi, 1)

            def hi_part_d(s, d):
                act.wait_ge(prod_d, s.d_before + d + 1)
                if some(s.q - (DEPTH - 1)):
                    act.wait_ge(used_d, s.q - (DEPTH - 1))
                act.activation(hi_d[:, s.slot, d, :], c_d[(s.d_par + d) % 2][:], ACT.Copy).then_inc(hi_d_ready, 1)

            def hi_parts_p(s):
                act.wait_ge(prod_p, s.q + 1)
                if some(s.q - (DEPTH - 1)):
                    act.wait_ge(used_p, s.q - (DEPTH - 1))
                act.activation(hi_p[:, s.slot, 0:s.g.P, :], c_p[:, s.slot, 0:s.g.P, :],
                               ACT.Copy).then_inc(hi_p_ready, 1)

            def relu_0(t, q_last, q_copied):
                act.wait_ge(used_p, q_last + 1)
                if q_copied is not None:
                    act.wait_ge(A_ready, q_copied + 1)
                    act.wait_ge(sum0, t)
                act.activation(k_stack[0:HID, :], z0[0:HID, :], ACT.Relu, bias=biases[0:HID, 0:1])
                act.activation(r0[:], z0[:], ACT.Relu, bias=biases[:, 0:1]).then_inc(relu0, 1)

            def relu_1(n, odd, q_last):
                act.wait_ge(used_p, q_last + 1)
                if some(n):
                    act.wait_ge(sum1, n)
                act.activation(r1[:], z1[odd][:], ACT.Relu, bias=biases[:, 1:2]).then_inc(relu1, 1)

            act.wait_ge(w0_summed, 1)
            act.activation(w_hi[0][:], w_full[0][:], ACT.Copy).then_inc(w_hi_ready, 1)
            split_x(0, 0)
            split_x(0, 1)

            def hi_parts_rest(s):
                hi_parts_p(s)
                for d in range(1, s.g.D):
                    hi_part_d(s, d)

            for s in start_steps():
                hi_part_d(s, 0)
                hi_parts_rest(s)

            def period(i, odd):
                n = 2 * i + odd
                last = is_at_least(i, odd, TILES - 1)
                steps = period_steps(n, odd, order_of(n))
                first = not some(n)

                for k, s in enumerate(steps):
                    hi_part_d(s, 0)
                    if s.pos == 5 and not last:
                        relu_0(n + 1, steps[order_of(n).index(3)].q, s.q)
                    hi_parts_rest(s)
                    if k == 2 and not first:
                        relu_1(n - 1, 1 - odd, steps[0].q - 1)
                    if k == 0 and not is_at_least(i, odd, TILES - 2):
                        split_x(i + 1, odd)
                    if k == 0 and first:
                        act.wait_ge(bias_in, 16)
                        relu_0(0, len(START) - 1, None)
                        act.wait_ge(w1_in, 16)
                        for lot in W1_LOTS:
                            act.activation(w_hi[1][:, lot, :], w_full[1][:, lot, :], ACT.Copy).then_inc(w_hi_ready, 1)

            all_periods(act, period)
            end = period_steps(TILES - 1, 1, LAST)
            relu_1(TILES - 1, 1, end[-1].q)
            act.wait_ge(mlp_in, 16 * 5)
            for m in range(M1):
                act.wait_ge(h1_psum, m + 1)
                act.activation(h1[:, m, :], h1_banks[m][:], ACT.Relu,
                               bias=biases[:, 2 + m:3 + m]).then_inc(h1_ready, 1)
            for m in range(M2):
                act.wait_ge(h2_psum, m + 1)
                act.activation(h2[:, m, :], h2_banks[m][:], ACT.Relu,
                               bias=biases[:, 2 + M1 + m:3 + M1 + m]).then_inc(h2_ready, 1)
            act.wait_ge(y_psum, 1)
            act.activation(y_sb[:], c_d[1][0:1, :], ACT.Copy).then_inc(y_ready, 1)

        @block.vector
        def _(dve):
            dve.memset(x_stack[:].bitcast(F32), 0.0).then_inc(zeroed, 1)
            dve.memset(s0[0:HID, :], 0.0).then_inc(zeroed, 1)

            def split_x(t, odd):
                dve.wait_ge(x_hi, t + 1)
                dve.tensor_tensor(gathered_parts[:, odd, 1, :], gathered[:, odd, :],
                                  gathered_parts[:, odd, 0, :].bitcast(F32), ALU.subtract).then_inc(x_lo, 1)

            def products(s, fresh=None):
                dve.wait_ge(A_ready, s.q + 1)
                a = A[s.par][:]

                def wait_B(upto):
                    if fresh is not None:
                        dve.wait_ge(B_in[s.tile][0], 16 * fresh)
                        if upto > B_PARTS[0][1]:
                            dve.wait_ge(B_in[s.tile][1], 16 * fresh)

                def product_d(d):
                    if some(s.d_before + (d - 1)):
                        dve.wait_ge(lo_d_ready, s.d_before + (d - 1))
                    dve.tensor_tensor(c_d[(s.d_par + d) % 2][:], B[:, s.tile, d, :], a, ALU.mult).then_inc(prod_d, 1)

                def lo_part_d(d):
                    dve.wait_ge(hi_d_ready, s.d_before + d + 1)
                    if some(s.q - (DEPTH - 1)):
                        dve.wait_ge(used_d, s.q - (DEPTH - 1))
                    dve.tensor_tensor(lo_d[:, s.slot, d, :], c_d[(s.d_par + d) % 2][:],
                                      hi_d[:, s.slot, d, :].bitcast(F32), ALU.subtract).then_inc(lo_d_ready, 1)

                wait_B(s.g.D + s.g.P)
                product_d(0)
                wide = a.rearrange("p (o n) -> p o n", o=1)
                if some(s.p_freed):
                    dve.wait_ge(lo_p_ready, s.p_freed)
                dve.tensor_tensor(c_p[:, s.slot, 0:s.g.P, :], B[:, s.tile, s.g.D:s.g.D + s.g.P, :],
                                  wide.to_broadcast([128, s.g.P, N]), ALU.mult).then_inc(prod_p, 1)
                for d in range(1, s.g.D):
                    product_d(d)
                if some(s.q - (DEPTH - 1)):
                    dve.wait_ge(used_f, s.q - (DEPTH - 1))
                first_f = s.g.D + s.g.P
                wait_B(first_f + s.g.F)
                dve.tensor_tensor(c_f[:, s.slot, 0:s.g.F, :], B[:, s.tile, first_f:first_f + s.g.F, :],
                                  wide.to_broadcast([128, s.g.F, N]), ALU.mult).then_inc(prod_f, 1)
                for d in range(s.g.D):
                    lo_part_d(d)

            def split_k_and_sum_0(t, column):
                dve.wait_ge(relu0, t + 1)
                dve.tensor_tensor(k_stack[HID:, :], r0[0:HID, :], k_stack[0:HID, :].bitcast(F32),
                                  ALU.subtract).then_inc(k_lo, 1)
                dve.tensor_reduce(s0[HID:, bass.ds(column, TB)], r0[HID:, :].rearrange("p (b k) -> p b k", k=K),
                                  AX_X, ALU.add).then_inc(sum0, 1)

            def sum_1(n, column):
                dve.wait_ge(relu1, n + 1)
                dve.tensor_reduce(s1[:, bass.ds(column, TB)], r1[:].rearrange("p (b k) -> p b k", k=K),
                                  AX_X, ALU.add).then_inc(sum1, 1)

            dve.wait_ge(w0_fg_in, 16)
            dve.wait_ge(w0_gf_in, 16)
            dve.tensor_tensor(w_full[0][:], w_full[0][:], gf_raw, ALU.add).then_inc(w0_summed, 1)
            dve.wait_ge(w0_summed, 1)
            dve.wait_ge(w_hi_ready, 1)
            dve.tensor_tensor(w_lo[0][:], w_full[0][:], w_hi[0][:].bitcast(F32), ALU.subtract).then_inc(w_lo_ready, 1)

            def lo_part_w1(j):
                lot = W1_LOTS[j]
                dve.wait_ge(w_hi_ready, 2 + j)
                dve.tensor_tensor(w_lo[1][:, lot, :], w_full[1][:, lot, :], w_hi[1][:, lot, :].bitcast(F32),
                                  ALU.subtract).then_inc(w_lo_ready, 1)

            split_x(0, 0)
            dve.wait_ge(sel_ready, 1)
            first, second = start_steps()
            split_x(1, 1)
            products(first, 1)
            products(second)

            def period(i, odd):
                n = 2 * i + odd
                for k, s in enumerate(period_steps(n, odd, order_of(n))):
                    products(s, i + (1 + odd) if s.pos == 2 else None)
                    if k == 0 and not some(n):
                        split_k_and_sum_0(0, 0)
                        lo_part_w1(0)
                        lo_part_w1(1)
                    if k == 1 and not some(n):
                        lo_part_w1(2)
                        lo_part_w1(3)
                    if k == 3 and some(n):
                        sum_1(n - 1, (n - 1) * TB)
                    if k == 1 and not is_at_least(i, odd, TILES - 2):
                        split_x(n + 2, odd)
                    if s.pos == 5 and not is_at_least(i, odd, TILES - 1):
                        split_k_and_sum_0(n + 1, (n + 1) * TB)

            all_periods(dve, period)
            sum_1(TILES - 1, (TILES - 1) * TB)

        @block.tensor
        def _(pe):
            def x_placed(t_half, odd):
                pe.wait_ge(x_in[odd], 2 * 16 * (t_half + 1))

            def copy_A(s, t, placed=None):
                if some(s.q - 1):
                    pe.wait_ge(prod_f, s.q - 1)
                if s.g.layer == 0:
                    if placed is not None:
                        x_placed(*placed)
                    pe.matmul(A[s.par][:], sel[0:XROWS, SEL_A0 + s.g.j, :], x_stack[0:XROWS, s.tile, :],
                              start=True, stop=True).then_inc(A_ready, 1)
                else:
                    pe.wait_ge(k_lo, t + 1)
                    pe.matmul(A[s.par][:], sel[:, SEL_A1 + s.g.j, :], k_stack[:],
                              start=True, stop=True).then_inc(A_ready, 1)

            def chunks(s, between=None):
                layer, g = s.g.layer, s.g
                z = z1[s.tile] if layer else z0
                opens = g.j == 0
                closes = g.j == (NJ1 - 1 if layer else 1)
                for f in range(g.F):
                    i = g.D + g.P + f
                    if f == 0:
                        pe.wait_ge(prod_f, s.q + 1)
                    last = pe.matmul(z[:], w_full[layer][:, NB * g.j + i, :], c_f[:, s.slot, f, :],
                                     start=opens and f == 0, stop=False)
                    if f == g.F - 1:
                        last.then_inc(used_f, 1)
                    if between:
                        between()
                for kind, count, hi, lo, before, ready, used in (
                        ("D", g.D, hi_d, lo_d, s.d_before, lo_d_ready, used_d),
                        ("P", g.P, hi_p, lo_p, s.p_before, lo_p_ready, used_p)):
                    for c in range(count):
                        i = c + (g.D if kind == "P" else 0)
                        pe.wait_ge(ready, before + c + 1)
                        w = NB * g.j + i
                        pe.matmul(z[:], w_hi[layer][:, w, :], hi[:, s.slot, c, :], start=False, stop=False)
                        pe.matmul(z[:], w_hi[layer][:, w, :], lo[:, s.slot, c, :], start=False, stop=False)
                        ends = c == count - 1
                        last = pe.matmul(z[:], w_lo[layer][:, w, :], hi[:, s.slot, c, :], start=False,
                                         stop=closes and kind == "P" and ends)
                        if ends:
                            last.then_inc(used, 1)
                        if between:
                            between()

            pe.wait_ge(sel_ready, 1)
            first, second = start_steps()
            copy_A(first, 0, (0, 0))
            copy_A(second, 0)
            for _ in range(WARM_UP):
                pe.matmul(spare[:], sel[:, 0, :], sel[:, 0:N // 128, :].rearrange("p s l -> p (s l)"),
                          start=True, stop=True)
            pe.wait_ge(w_lo_ready, 1)
            chunks(first)
            ahead = period_steps(0, 0, FIRST)
            copy_A(ahead[0], 1, (0, 1))
            chunks(second)
            copy_A(ahead[1], 1)

            def start_mlp(s):
                pe.wait_ge(sum0, TILES)
                pe.wait_ge(dense_in, 16)
                pe.wait_ge(mlp_in, 16 * 5)
                pe.wait_ge(relu0, TILES)
                pe.wait_ge(relu1, TILES - 1)
                pe.wait_ge(prod_f, s.q)
                for m in range(M1):
                    pe.matmul(h1_banks[m][:], wt1_sb[:, 0, m * 128:(m + 1) * 128], s0[:], start=True, stop=False)

            def period(i, odd):
                n = 2 * i + odd
                steps = period_steps(n, odd, order_of(n))
                last = is_at_least(i, odd, TILES - 1)
                targets = [(s, n) if s.g.layer else (s, n + 1, (i + odd, 1 - odd)) for s in steps[2:]]
                if not last:
                    targets += [(s, n + 1) for s in period_steps(n + 1, 1 - odd, order_of(n + 1))[:2]]
                for k, s in enumerate(steps):
                    target = targets[k] if k < len(targets) else None
                    after = MAKES.get(s.pos) if not last else None
                    if order_of(n) is FIRST and k == 0:
                        after = FIRST_MAKES
                    if target and after is None:
                        copy_A(*target)
                    if s.pos == 0 and some(n - 1):
                        pe.wait_ge(relu1, n - 1)
                    if s.pos == 2:
                        pe.wait_ge(relu0, n + 1)
                    if s.pos == 0 and not some(n):
                        pe.wait_ge(w_lo_ready, 1 + NJ1)
                    if s.pos == 5 and last:
                        start_mlp(s)
                    done = iter(range(1, NB + 1))

                    def make():
                        if next(done) == after:
                            copy_A(*target)

                    chunks(s, make)

            all_periods(pe, period)

            pe.wait_ge(sum1, TILES)
            for m in range(M1):
                pe.matmul(h1_banks[m][:], wt1_sb[:, 1, m * 128:(m + 1) * 128], s1[:], start=False,
                          stop=True).then_inc(h1_psum, 1)
            for m in range(M2):
                for c in range(M1):
                    if m == 0:
                        pe.wait_ge(h1_ready, c + 1)
                    last = pe.matmul(h2_banks[m][:], wt2_sb[:, c, m * 128:(m + 1) * 128], h1[:, c, :],
                                     start=c == 0, stop=c == M1 - 1)
                last.then_inc(h2_psum, 1)
            for m in range(M2):
                pe.wait_ge(h2_ready, m + 1)
                last = pe.matmul(c_d[1][0:1, :], wt3_sb[:, m:m + 1], h2[:, m, :], start=m == 0, stop=m == M2 - 1)
            last.then_inc(y_psum, 1)


def kernel(**inputs):
    import concourse.bacc as _bacc
    from concourse.bass_utils import run_bass_kernel_spmd as _run

    tables = [np.asarray(inputs[f"tbl_{f}"]) for f in range(NF)]
    sizes = [t.shape[0] for t in tables]
    starts = np.concatenate([[0], np.cumsum(sizes)[:-1]]).astype(np.int32)

    def by_lane(a):
        a = a.reshape(TILES, TB, GATHERS, FPG)
        return np.ascontiguousarray(a.transpose(3, 1, 0, 2).reshape(128, TILES * GATHERS))

    fg, gf = pair_lanes()
    w0 = np.asarray(inputs["L0_rec_W0"])
    w0 = np.concatenate([w0, np.zeros((1, C0), w0.dtype)])
    w1 = np.asarray(inputs["L0_rec_W1"]).reshape(128 // NG, NB, NG, NJ1, C0)
    wt1 = np.asarray(inputs["W_top1"])
    nz = HID + C0
    arrays = {
        "tables": np.concatenate(tables),
        "ids": by_lane(np.asarray(inputs["ids"])),
        "id_base": by_lane(np.broadcast_to(starts, (BATCH, NF))),
        "select": selections(),
        "w0_fg": w0[fg.T],
        "w0_gf": w0[gf.T],
        "w1": w1.transpose(0, 2, 3, 1, 4).reshape(128, CH1, C0),
        "bias": np.stack([np.asarray(inputs["L0_rec_b0"]), np.asarray(inputs["L0_rec_b1"])], axis=1),
        "dense_t": np.asarray(inputs["dense_ctx"]).T,
        "wt1": np.concatenate([wt1[nz:], np.zeros((HID - ND, N1), wt1.dtype), wt1[:HID], wt1[HID:nz]]),
        "bt1": np.asarray(inputs["b_top1"]).reshape(M1, 128).T,
        "wt2": np.asarray(inputs["W_top2"]),
        "bt2": np.asarray(inputs["b_top2"]).reshape(M2, 128).T,
        "wt3": np.asarray(inputs["W_top3"]).reshape(M2, 128).T,
    }
    nc = _bacc.Bacc("TRN2", target_bir_lowering=False, num_devices=1)
    args = []
    for name, a in arrays.items():
        arrays[name] = a = np.ascontiguousarray(a)
        args.append(nc.dram_tensor(name, a.shape, mybir.dt.from_np(a.dtype), kind="ExternalInput").ap())
    args.append(nc.dram_tensor("y", (BATCH, 1), F32, kind="ExternalOutput").ap().rearrange("b o -> o b"))
    tower_kernel(nc, *args)
    r = _run(nc, [arrays], core_ids=[0])
    return r.results[0]["y"]
```
